# Optimizing a Trainium2 kernel written in Bass

```python
import numpy as np
import jax
import jax.numpy as jnp

def _softmax(x, axis=-1):
    return jax.nn.softmax(x, axis=axis)

def _gelu(x):
    return jax.nn.gelu(x, approximate=True)

def _silu(x):
    return jax.nn.silu(x)

def _sigmoid(x):
    return jax.nn.sigmoid(x)

def _layernorm(x, axis=-1, eps=1e-05):
    m = jnp.mean(x, axis=axis, keepdims=True)
    v = jnp.var(x, axis=axis, keepdims=True)
    return (x - m) / jnp.sqrt(v + eps)

def _scatter_add(tgt, idx, src, axis=0):
    return tgt.at[idx].add(src)

def _segment_sum(src, seg, n):
    return jax.ops.segment_sum(src, seg, n)
kernel_name = 'mk_adj_resnorm_d1_adj_r2_fb9445'

def setup_inputs(seed: int=0):
    np.random.seed(seed)
    _w = jnp.asarray

    def _rec_inputs():
        import jax
        import jax.numpy as jnp
        _gk = jax.random.key(seed)
        x = -9.806e-05 + 1 * jax.random.normal(jax.random.fold_in(_gk, 1), (4096, 64), jnp.float32)
        _w = (1.0 + jnp.arange(4096, dtype=jnp.float32)) ** (-0.5)
        _w = _w / _w.mean()
        _pij = jnp.clip(0.000488281 * _w[:, None] * _w[None, :], 0.0, 1.0)
        _a = jax.random.uniform(jax.random.fold_in(_gk, 2), (4096, 4096)) < _pij
        adj = _a.astype(jnp.int32)
        return (x, adj)
    x, adj = _rec_inputs()

    def _L0_gnn_setup():
        import jax, jax.numpy as jnp
        import numpy as np
        ALPHA = 0.2
        NEG_BIG = -9000000000000000.0
        key = jax.random.key(seed)
        k1, k2, k3, k4, k5 = jax.random.split(key, 5)
        N, M, F_in, F_out = (4096, 4096, 64, 64)
        item_embs = jax.random.normal(k1, (N, F_in), dtype=jnp.float32)
        entity_embs = jax.random.normal(k2, (M, F_in), dtype=jnp.float32)
        adj = jax.random.randint(k3, (N, M), 0, 2, dtype=jnp.int32)
        W = jax.random.normal(k4, (F_in, F_out), dtype=jnp.float32)
        a = jax.random.normal(k5, (2 * F_out, 1), dtype=jnp.float32)
        return {'item_embs': item_embs, 'entity_embs': entity_embs, 'adj': adj, 'W': W, 'a': a}
    _L0_gnn_all = _L0_gnn_setup()
    _L0_gnn_in = {k: v for k, v in _L0_gnn_all.items() if k in ('entity_embs', 'W', 'a')}
    del _L0_gnn_all
    return {'x': x, 'adj': adj, 'L0_gnn_entity_embs': _L0_gnn_in['entity_embs'], 'L0_gnn_W': _L0_gnn_in['W'], 'L0_gnn_a': _L0_gnn_in['a']}

def reference(x, adj, L0_gnn_entity_embs, L0_gnn_W, L0_gnn_a):
    import jax
    import jax.numpy as jnp

    def _L0_gnn_ref(item_embs, entity_embs, adj, W, a):
        import jax, jax.numpy as jnp
        import numpy as np
        ALPHA = 0.2
        NEG_BIG = -9000000000000000.0
        F_out = W.shape[1]
        Wh = item_embs @ W
        We = entity_embs @ W
        a1 = a[:F_out, 0]
        a2 = a[F_out:, 0]
        scores = (Wh @ a1)[:, None] + (We @ a2)[None, :]
        e = jnp.where(scores > 0, scores, ALPHA * scores)
        e = jnp.where(adj > 0, e, NEG_BIG)
        attention = jax.nn.softmax(e, axis=1)
        entity_emb_weighted = attention @ entity_embs
        h_prime = entity_emb_weighted + item_embs
        return jax.nn.elu(h_prime)
    x = _layernorm(x + _L0_gnn_ref(x, L0_gnn_entity_embs, adj, L0_gnn_W, L0_gnn_a), axis=-1)
    return x

_drawn_inputs = setup_inputs


def setup_inputs(seed=0):
    import zlib

    import numpy as np

    out = dict(_drawn_inputs(seed))
    spreads = {}
    factors = {}
    for name, (base, spread) in spreads.items():
        noise = np.random.default_rng([zlib.crc32(name.encode()), seed]).standard_normal(out[name].shape)
        drawn = base * np.exp(spread * noise) if base else spread * noise
        out[name] = jnp.asarray(drawn.astype(out[name].dtype))
    for name, factor in factors.items():
        out[name] = (out[name] * factor).astype(out[name].dtype)
    return out
```

```python
import numpy as np
import concourse.bass as bass
from concourse import mybir
from contextlib import ExitStack

P = 128
N, M, F = 4096, 4096, 64
T = 8
SR = T * P
NG = N // SR
NT = N // P
NB = M // P
NP = NB // 2
H = M // 2
PH = 2 * NG
HB = NB // 2
V = 4
Q = M // 4
SLOTS = 4
FA = F + 1
ALPHA = 0.2
BIG = 8192.0
EPS = 1e-5


def attention_layernorm(nc, x, adj, ent, xT, entT, wT, aT, out):
    fp32, bf16, i32 = mybir.dt.float32, mybir.dt.bfloat16, mybir.dt.int32
    ALU, ACT, AX = mybir.AluOpType, mybir.ActivationFunctionType, mybir.AxisListType

    adj_t = adj.rearrange("(g p t) m -> g t p m", g=NG, p=P)
    x_g = x.rearrange("(g p t) f -> g p t f", g=NG, p=P)
    out_g = out.rearrange("(g p t) f -> g p t f", g=NG, p=P)

    ctx = ExitStack()
    with ctx:
        def sb(name, shape, dt):
            return ctx.enter_context(nc.sbuf_tensor(name, shape, dt))

        def sem(name):
            return ctx.enter_context(nc.semaphore(name))

        adj_sb = sb("adj_sb", [P, SLOTS, Q], i32)
        mask = sb("mask", [P, 3, T, H], bf16)
        qn = sb("qn", [P, M], bf16)
        found = sb("found", [P, H], bf16)
        pb = sb("pb", [P, N], fp32)
        ent_sb = sb("ent_sb", [P, NB, FA], fp32)
        x_sb = sb("x_sb", [P, T, F], fp32)
        leaky = sb("leaky", [P, 2, 2 * SR], fp32)
        wts = sb("wts", [P, 2, 2 * SR], fp32)
        diag = sb("diag", [P, 2, T, P], bf16)
        ident = sb("ident", [P, P], bf16)
        wT_sb = sb("wT_sb", [F, F], fp32)
        aT_sb = sb("aT_sb", [F, 2], fp32)
        wa = sb("wa", [F, 2], fp32)
        wa1_rep = sb("wa1_rep", [F, P], fp32)
        wa2_rep = sb("wa2_rep", [F, P], fp32)
        onesf = sb("onesf", [P, P], fp32)
        zrow = sb("zrow", [1, T // 2 * FA], bf16)
        qcol = sb("qcol", [P, NB], fp32)
        q_hi = sb("q_hi", [P, NB], fp32)
        q_lo = sb("q_lo", [P, NB], fp32)
        pcol = sb("pcol", [P, NT], fp32)
        qm = sb("qm", [P, 2], fp32)
        qg = sb("qg", [P, 2], fp32)
        qrange = sb("qrange", [P, 1], fp32)
        qinv = sb("qinv", [P, 1], fp32)
        qoff = sb("qoff", [P, 1], fp32)
        qmin = sb("qmin", [P, 1], fp32)
        top = sb("top", [P, 2, NT], fp32)
        empty = sb("empty", [P, NT], fp32)
        st = sb("st", [P, 4, T], fp32)
        ent_sum = sb("ent_sum", [P, FA], fp32)
        h = sb("h", [P, T, FA], fp32)
        e = sb("e", [P, T, F], fp32)
        y = sb("y", [P, T, F], fp32)
        rinv = sb("rinv", [P, T], fp32)
        mean = sb("mean", [P, T], fp32)
        var = sb("var", [P, T], fp32)
        rstd = sb("rstd", [P, T], fp32)
        mhalf = sb("mhalf", [P, T], fp32)
        y_out = sb("y_out", [P, T, F], fp32)

        turned = mask[0:F, 2, :, :].rearrange("p t m -> p (t m)").bitcast(fp32)
        xT_sb, entT_sb = turned[:, 0:N], turned[:, N:N + M]

        X = [ctx.enter_context(nc.psum_tensor(f"X{i}", [P, SR], fp32)) for i in range(2)]
        acc = [ctx.enter_context(nc.psum_tensor(f"acc{i}", [P, 512], fp32)) for i in range(2)]
        S = [ctx.enter_context(nc.psum_tensor(f"S{i}", [P, 512], fp32)) for i in range(2)]

        w_in = sem("w_in")
        xT_in = sem("xT_in")
        entT_in = sem("entT_in")
        ent_in = sem("ent_in")
        adj_in = [sem(f"adj_in{i}") for i in range(SLOTS)]
        x_in = sem("x_in")
        out_done = sem("out_done")
        ident_done = sem("ident_done")
        const_done = sem("const_done")
        wa_mm = sem("wa_mm")
        wa_done = sem("wa_done")
        cols_mm = sem("cols_mm")
        cols_done = sem("cols_done")
        qmax_done = sem("qmax_done")
        q_all = sem("q_all")
        q_step = sem("q_step")
        q_parts = sem("q_parts")
        rep_done = sem("rep_done")
        row_mm = sem("row_mm")
        q_rows = sem("q_rows")
        p_rows = sem("p_rows")
        sum_mm = sem("sum_mm")
        sum_done = sem("sum_done")
        top_done = sem("top_done")
        mask_done = sem("mask_done")
        st_step = sem("st_step")
        diag_done = sem("diag_done")
        x_done = sem("x_done")
        leaky_done = sem("leaky_done")
        z_done = sem("z_done")
        w_done = sem("w_done")
        w_used = sem("w_used")
        acc_free = sem("acc_free")
        ep_step = sem("ep_step")
        neg_done = sem("neg_done")
        exp_done = sem("exp_done")
        var_done = sem("var_done")
        rstd_done = sem("rstd_done")
        y_done = sem("y_done")

        block = ctx.enter_context(nc.Block())
        qneg = top[:, 0, 0:NB]

        def steps(eng, f, body, head=None):
            body(f, 0)
            if head:
                head()
            with eng.Fori(1, V) as v:
                body(f, v)

        def load(sp, f, v):
            for c in range(SLOTS):
                if not (f == 0 and isinstance(v, int)):
                    sp.wait_ge(mask_done, SLOTS * (V * f + v - 1) + c + 1)
                col = H * (f % 2) + Q * (c % 2)
                sp.dma_start(adj_sb[:, c, :], adj_t[f // 2, 2 * v + c // 2, :, col:col + Q]).then_inc(adj_in[c], 16)

        def store(sp, g):
            sp.wait_ge(y_done, g + 1)
            sp.dma_start(out_g[g], y_out[:, :, :]).then_inc(out_done, 16)
            if g + 1 < NG:
                sp.dma_start(x_sb[:, :, :], x_g[g + 1]).then_inc(x_in, 16)

        def inverse_std(pool, g):
            pool.wait_ge(var_done, g + 1)
            pool.tensor_tensor(rstd[:, :], var[:, :], mhalf[:, :], ALU.pow).then_inc(rstd_done, 1)

        def elu_exp(act, g):
            act.wait_ge(neg_done, g + 1)
            act.activation(e[:, :, :], e[:, :, :], ACT.Exp).then_inc(exp_done, 1)

        @block.sync
        def _(sp):
            sp.dma_start(wT_sb[:, :], wT).then_inc(w_in, 16)
            sp.dma_start(aT_sb[:, :], aT).then_inc(w_in, 16)
            sp.dma_start(entT_sb, entT).then_inc(entT_in, 16)
            load(sp, 0, 0)
            sp.dma_start(xT_sb, xT).then_inc(xT_in, 16)
            with sp.Fori(1, V) as v:
                load(sp, 0, v)
            sp.dma_start(ent_sb[:, :, 0:F], ent.rearrange("(b p) f -> p b f", p=P)).then_inc(ent_in, 16)
            sp.dma_start(x_sb[:, :, :], x_g[0]).then_inc(x_in, 16)
            for f in range(1, PH):
                with sp.Fori(0, V) as v:
                    load(sp, f, v)
                if f >= 5 and f % 2 == 1:
                    store(sp, (f - 5) // 2)
            for g in range((PH - 4) // 2, NG):
                store(sp, g)
            sp.wait_ge(out_done, 16 * NG)

        @block.gpsimd
        def _(pool):
            pool.memset(ident[:, :], 0.0).then_inc(ident_done, 1)
            pool.wait_ge(ident_done, 1)
            pool.affine_select(out=ident[:, :], in_=ident[:, :], compare_op=ALU.not_equal, fill=1.0,
                               base=0, pattern=[[-1, P]], channel_multiplier=1).then_inc(ident_done, 1)
            pool.wait_ge(qmax_done, 2)
            pool.partition_all_reduce(qg[:, :], qm[:, :], P, bass.bass_isa.ReduceOp.max).then_inc(q_all, 1)

            def make_masks(f, v):
                for c in range(SLOTS):
                    pool.wait_ge(adj_in[c], 16 * (V * f + v + 1))
                    pool.tensor_scalar(mask[:, f % 3, 2 * v + c // 2, Q * (c % 2):Q * (c % 2) + Q], adj_sb[:, c, :],
                                       1.0, 0.0, ALU.min, ALU.max).then_inc(mask_done, 1)

            for f in range(PH):
                if f == 2:
                    pool.wait_ge(cols_mm, 2)
                if f >= 3:
                    pool.wait_ge(x_done, HB * (f - 2))
                for v in range(V):
                    make_masks(f, v)
                if f >= 4 and f % 2 == 0:
                    inverse_std(pool, f // 2 - 2)
            for g in range((PH - 4) // 2, NG):
                inverse_std(pool, g)

        @block.scalar
        def _(act):
            for c in range(8):
                act.wait_ge(row_mm, 9 + c)
                act.activation(pb[:, 512 * c:512 * c + 512], S[c % 2][:, :], ACT.Copy).then_inc(p_rows, 1)
            act.wait_ge(p_rows, 8)
            act.wait_ge(q_parts, 1)

            def weights(slot, block):
                for b in range(2):
                    part = wts[:, slot, SR * b:SR * b + SR]
                    act.activation(part, part, ACT.Exp, bias=q_lo[:, bass.ds(block + b, 1)]).then_inc(w_done, 1)

            def scores(f, v):
                for c in range(2):
                    k = HB // 2 * f + 2 * v + c
                    if not (f == 0 and isinstance(v, int)):
                        act.wait_ge(z_done, 2 * k - 2)
                        weights(c, (HB * (f % 2) - 4 + NB) % NB + 2 * c if isinstance(v, int)
                                else HB * (f % 2) + 4 * v + 2 * c - 4)
                    for b in range(2):
                        act.activation(leaky[:, c, SR * b:SR * b + SR], pb[:, SR * (f // 2):SR * (f // 2) + SR],
                                       ACT.Relu, bias=q_hi[:, bass.ds(HB * (f % 2) + 4 * v + 2 * c + b, 1)],
                                       scale=1 - ALPHA).then_inc(leaky_done, 1)

            for f in range(PH):
                steps(act, f, scores)
                if f % 2 == 0 and f >= 2:
                    elu_exp(act, f // 2 - 1)
            for k in range(NP * NG - 2, NP * NG):
                act.wait_ge(z_done, 2 * k + 2)
                weights(k % 2, 2 * (k % NP))
            elu_exp(act, NG - 1)

        @block.vector
        def _(dve):
            dve.memset(onesf[:, :], 1.0)
            dve.memset(zrow[:, :], 0.0)
            dve.memset(mhalf[:, :], -0.5)
            dve.memset(ent_sb[:, :, F:FA], 1.0).then_inc(const_done, 1)
            dve.wait_ge(wa_mm, 1)
            dve.tensor_copy(wa[:, :], S[0][0:F, 0:2]).then_inc(wa_done, 1)
            dve.wait_ge(cols_mm, 1)
            dve.tensor_copy(qcol[:, :], S[1][:, 0:NB]).then_inc(cols_done, 1)
            dve.wait_ge(cols_done, 1)
            dve.tensor_reduce(qm[:, 0:1], qcol[:, :], AX.X, ALU.max).then_inc(qmax_done, 1)
            dve.tensor_scalar(q_hi[:, :], qcol[:, :], 1 - ALPHA, None, ALU.mult)
            dve.tensor_scalar(q_lo[:, :], qcol[:, :], ALPHA, None, ALU.mult).then_inc(q_parts, 1)
            dve.tensor_scalar(qneg, qcol[:, :], -1.0, None, ALU.mult).then_inc(q_step, 1)
            dve.wait_ge(q_step, 1)
            dve.tensor_reduce(qm[:, 1:2], qneg, AX.X, ALU.max).then_inc(qmax_done, 1)
            dve.wait_ge(q_all, 1)
            dve.tensor_scalar(qmin[:, :], qg[:, 1:2], -1.0, None, ALU.mult)
            dve.scalar_tensor_tensor(qrange[:, :], qg[:, 0:1], 1e-3, qg[:, 1:2], ALU.add, ALU.add).then_inc(q_step, 1)
            dve.wait_ge(q_step, 2)
            dve.tensor_scalar(qrange[:, :], qrange[:, :], 1.02, None, ALU.mult).then_inc(q_step, 1)
            dve.wait_ge(q_step, 3)
            dve.reciprocal(qinv[:, :], qrange[:, :]).then_inc(q_step, 1)
            dve.wait_ge(q_step, 4)
            dve.tensor_tensor(qoff[:, :], qg[:, 1:2], qinv[:, :], ALU.mult).then_inc(q_step, 1)
            dve.tensor_scalar(wa2_rep[:, :], onesf[0:F, :], wa[:, 1:2], qinv[0:F, :], ALU.mult,
                              ALU.mult).then_inc(rep_done, 1)
            dve.tensor_scalar(wa1_rep[:, :], onesf[0:F, :], wa[:, 0:1], None, ALU.mult).then_inc(rep_done, 1)
            dve.wait_ge(q_step, 5)
            for c in range(8):
                dve.wait_ge(row_mm, 1 + c)
                dve.tensor_scalar(qn[:, 512 * c:512 * c + 512], S[c % 2][:, :], qoff[:, :], 2.0 ** -7, ALU.add,
                                  ALU.max).then_inc(q_rows, 1)
            dve.wait_ge(q_rows, 8)

            def search(f, t):
                dve.wait_ge(mask_done, 2 * (T * f + t + 1))
                if T * f + t:
                    dve.wait_ge(top_done, T * f + t)
                dve.tensor_tensor_reduce(out=found[:, :], in0=mask[:, f % 3, t, :], in1=qn[:, H * (f % 2):H * (f % 2) + H],
                                         scale=1.0, scalar=0.0, op0=ALU.mult, op1=ALU.max,
                                         accum_out=top[:, f % 2, T * (f // 2) + t:T * (f // 2) + t + 1]).then_inc(top_done, 1)

            def make_diag(g):
                s = slice(T * g, T * g + T)
                n = 6 * g
                dve.wait_ge(top_done, 2 * T * (g + 1))
                dve.tensor_tensor(st[:, 3], top[:, 0, s], top[:, 1, s], ALU.max).then_inc(st_step, 1)
                dve.wait_ge(st_step, n + 1)
                dve.tensor_scalar(empty[:, s], st[:, 3], 0.0, None, ALU.is_le)
                dve.tensor_scalar(st[:, 0], st[:, 3], qrange[:, :], qmin[:, :], ALU.mult, ALU.add).then_inc(st_step, 1)
                dve.wait_ge(st_step, n + 2)
                dve.tensor_tensor(st[:, 1], st[:, 0], pcol[:, s], ALU.add).then_inc(st_step, 1)
                dve.wait_ge(st_step, n + 3)
                dve.tensor_scalar(st[:, 2], st[:, 1], 0.0, 1 - ALPHA, ALU.max, ALU.mult).then_inc(st_step, 1)
                dve.wait_ge(st_step, n + 4)
                dve.scalar_tensor_tensor(st[:, 2], st[:, 0], ALPHA, st[:, 2], ALU.mult, ALU.add).then_inc(st_step, 1)
                dve.wait_ge(st_step, n + 5)
                dve.tensor_scalar(st[:, 3], st[:, 2], -1.0, BIG, ALU.mult, ALU.add).then_inc(st_step, 1)
                dve.wait_ge(st_step, n + 6)
                dve.tensor_tensor(diag[:, g % 2], ident[:, :].unsqueeze(1).to_broadcast([P, T, P]),
                                  st[:, 3].unsqueeze(2).to_broadcast([P, T, P]), ALU.mult).then_inc(diag_done, 1)

            def exponents(k):
                if k >= 2:
                    dve.wait_ge(w_used, k - 1)
                for b in range(2):
                    dve.wait_ge(x_done, 2 * k + b + 1)
                    dve.wait_ge(leaky_done, 2 * k + b + 1)
                    dve.scalar_tensor_tensor(wts[:, k % 2, SR * b:SR * b + SR], X[b][:, :], -BIG,
                                             leaky[:, k % 2, SR * b:SR * b + SR], ALU.add, ALU.add).then_inc(z_done, 1)

            def phase(f):
                for t in range(T):
                    if f + 2 < PH:
                        search(f + 2, t)
                        if f % 2 == 1 and t == T - 1:
                            make_diag(f // 2 + 1)
                    if f % 2 == 0 and f >= 2 and t == 2:
                        take_sums(f // 2 - 1)
                    exponents(HB // 2 * f + t)
                    if f % 2 == 0 and f >= 2 and t == 2:
                        attend(f // 2 - 1)
                if f % 2 == 0 and f >= 2:
                    finish(f // 2 - 1)

            def take_sums(g):
                dve.wait_ge(w_used, NP * g + NP)
                for t in range(T):
                    ins = dve.scalar_tensor_tensor(h[:, t, :], ent_sum[:, :], empty[:, T * g + t:T * g + t + 1],
                                                   acc[t // (T // 2)][:, FA * (t % (T // 2)):FA * (t % (T // 2)) + FA],
                                                   ALU.mult, ALU.add)
                ins.then_inc(acc_free, 1)

            chained = [0]

            def chain(ins):
                chained[0] += 1
                ins.then_inc(ep_step, 1)
                dve.wait_ge(ep_step, chained[0])

            def spread(a):
                return a[:, :].unsqueeze(2).to_broadcast([P, T, F])

            def attend(g):
                dve.wait_ge(acc_free, g + 1)
                dve.wait_ge(x_in, 16 * (g + 1))
                chain(dve.reciprocal(rinv[:, :], h[:, :, F]))
                chain(dve.tensor_tensor(y[:, :, :], h[:, :, 0:F], spread(rinv), ALU.mult))
                chain(dve.tensor_tensor(y[:, :, :], y[:, :, :], x_sb[:, :, :], ALU.add))
                dve.tensor_scalar(e[:, :, :], y[:, :, :], 0.0, None, ALU.min).then_inc(neg_done, 1)
                chain(dve.scalar_tensor_tensor(y[:, :, :], y[:, :, :], 0.0, x_sb[:, :, :], ALU.max, ALU.add))

            def finish(g):
                dve.wait_ge(exp_done, g + 1)
                chain(dve.scalar_tensor_tensor(y[:, :, :], e[:, :, :], -1.0, y[:, :, :], ALU.add, ALU.add))
                chain(dve.tensor_reduce(mean[:, :], y[:, :, :], AX.X, ALU.add))
                chain(dve.tensor_scalar(mean[:, :], mean[:, :], 1.0 / F, None, ALU.mult))
                chain(dve.tensor_tensor(y[:, :, :], y[:, :, :], spread(mean), ALU.subtract))
                chain(dve.tensor_tensor(e[:, :, :], y[:, :, :], y[:, :, :], ALU.mult))
                chain(dve.tensor_reduce(var[:, :], e[:, :, :], AX.X, ALU.add))
                dve.tensor_scalar(var[:, :], var[:, :], 1.0 / F, EPS, ALU.mult, ALU.add).then_inc(var_done, 1)
                dve.wait_ge(rstd_done, g + 1)
                if g >= 1:
                    dve.wait_ge(out_done, 16 * g)
                dve.tensor_tensor(y_out[:, :, :], y[:, :, :], spread(rstd), ALU.mult).then_inc(y_done, 1)

            for f in range(2):
                for t in range(T):
                    search(f, t)
            dve.wait_ge(cols_mm, 2)
            dve.tensor_copy(pcol[:, :], S[1][:, NB:NB + NT]).then_inc(cols_done, 1)
            dve.wait_ge(sum_mm, 1)
            dve.tensor_copy(ent_sum[:, :], S[0][:, 0:FA]).then_inc(sum_done, 1)
            dve.wait_ge(cols_done, 2)
            dve.wait_ge(sum_done, 1)
            make_diag(0)
            for f in range(PH):
                phase(f)
            take_sums(NG - 1)
            attend(NG - 1)
            finish(NG - 1)

        @block.tensor
        def _(pe):
            pe.wait_ge(w_in, 32)
            pe.matmul(S[0][0:F, 0:2], wT_sb[:, :], aT_sb[:, :], start=True, stop=True).then_inc(wa_mm, 1)
            pe.wait_ge(wa_done, 1)
            pe.wait_ge(entT_in, 16)
            for b in range(NB):
                ins = pe.matmul(S[1][:, b:b + 1], entT_sb[:, P * b:P * b + P], wa[:, 1:2], start=True, stop=True)
            ins.then_inc(cols_mm, 1)
            pe.wait_ge(rep_done, 1)
            pe.wait_ge(cols_done, 1)
            for c in range(8):
                if c >= 2:
                    pe.wait_ge(q_rows, c - 1)
                pe.matmul(S[c % 2][:, :], wa2_rep[:, :], entT_sb[:, 512 * c:512 * c + 512],
                          start=True, stop=True).then_inc(row_mm, 1)
            pe.wait_ge(rep_done, 2)
            pe.wait_ge(xT_in, 16)
            for c in range(8):
                if c < 2:
                    pe.wait_ge(q_rows, 7 + c)
                else:
                    pe.wait_ge(p_rows, c - 1)
                pe.matmul(S[c % 2][:, :], wa1_rep[:, :], xT_sb[:, 512 * c:512 * c + 512],
                          start=True, stop=True).then_inc(row_mm, 1)
            pe.wait_ge(p_rows, 8)
            for t in range(NT):
                ins = pe.matmul(S[1][:, NB + t:NB + t + 1], xT_sb[:, P * t:P * t + P], wa[:, 0:1], start=True, stop=True)
            ins.then_inc(cols_mm, 1)
            pe.wait_ge(ent_in, 16)
            pe.wait_ge(const_done, 1)
            for b in range(NB):
                ins = pe.matmul(S[0][:, 0:FA], onesf[:, :], ent_sb[:, b, :], start=(b == 0), stop=(b == NB - 1))
            ins.then_inc(sum_mm, 1)
            pe.wait_ge(ident_done, 2)

            def turn(f, v, c, b):
                for t in range(T):
                    ins = pe.matmul(X[b][:, P * t:P * t + P], mask[:, f % 3, t, bass.ds((4 * v + 2 * c + b) * P, P)],
                                    diag[:, f // 2 % 2, t, :], start=True, stop=True)
                ins.then_inc(x_done, 1)

            def weigh(block, slot):
                for b in range(2):
                    for t in range(T):
                        ins = pe.matmul(acc[t // (T // 2)][:, FA * (t % (T // 2)):FA * (t % (T // 2)) + FA],
                                        wts[:, slot, SR * b + P * t:SR * b + P * t + P],
                                        ent_sb[:, block + b, :], start=False, stop=True, skip_group_check=True)
                ins.then_inc(w_used, 1)

            def step(f, v):
                head = isinstance(v, int)
                for c in range(2):
                    k = HB // 2 * f + 2 * v + c
                    for b in range(2):
                        if not (head and k == 0):
                            pe.wait_ge(z_done, 2 * k + b - 1)
                        turn(f, v, c, b)
                    if not (head and f == 0):
                        pe.wait_ge(w_done, 2 * k - 2)
                        weigh((HB * (f % 2) - 4 + NB) % NB + 2 * c if head else HB * (f % 2) + 4 * v + 2 * c - 4, c)

            def clear_acc(g):
                if g >= 1:
                    pe.wait_ge(acc_free, g)
                for a in acc:
                    pe.matmul(a[:, 0:T // 2 * FA], zrow[0:1, 0:P], zrow[0:1, :], start=True, stop=True)

            for f in range(PH):
                if f % 2 == 0:
                    pe.wait_ge(diag_done, f // 2 + 1)
                steps(pe, f, step, head=(lambda: clear_acc(f // 2)) if f % 2 == 0 else None)
            for c in range(2):
                pe.wait_ge(w_done, 2 * (NP * NG - 1 + c))
                weigh(NB - 4 + 2 * c, c)


def kernel(x, adj, L0_gnn_entity_embs, L0_gnn_W, L0_gnn_a):
    import concourse.bacc as bacc
    from concourse.bass_utils import run_bass_kernel_spmd

    x, adj, ent = np.asarray(x), np.asarray(adj), np.asarray(L0_gnn_entity_embs)
    w, a = np.asarray(L0_gnn_W), np.asarray(L0_gnn_a)
    xT = x.reshape(NG, P, T, F).transpose(3, 0, 2, 1).reshape(F, N)
    arrays = {"x": x, "adj": adj, "ent": ent, "xT": xT, "entT": ent.T, "wT": w.T, "aT": a.reshape(2, F).T}
    arrays = {k: np.ascontiguousarray(v) for k, v in arrays.items()}
    nc = bacc.Bacc("TRN2", target_bir_lowering=False, num_devices=1)
    args = {k: nc.dram_tensor(f"{k}_dram", v.shape, mybir.dt.from_np(v.dtype), kind="ExternalInput").ap()
            for k, v in arrays.items()}
    out = nc.dram_tensor("out_dram", (N, F), mybir.dt.float32, kind="ExternalOutput").ap()
    attention_layernorm(nc, **args, out=out)
    r = run_bass_kernel_spmd(nc, [{f"{k}_dram": v for k, v in arrays.items()}], core_ids=[0])
    return r.results[0]["out_dram"]
```

```python
import numpy as np
import concourse.bass as bass
from concourse import mybir
from contextlib import ExitStack

P = 128
N, M, F = 4096, 4096, 64
T = 8
SR = T * P
NG = N // SR
NT = N // P
NB = M // P
NP = NB // 2
H = M // 2
PH = 2 * NG
HB = NB // 2
V = 4
RING = 3 * T + T // 2
AHEAD = 4
FA = F + 1
ALPHA = 0.2
BIG = 8192.0
EPS = 1e-5


def attention_layernorm(nc, x, adj, ent, xT, entT, wT, aT, out):
    fp32, bf16, i32 = mybir.dt.float32, mybir.dt.bfloat16, mybir.dt.int32
    ALU, ACT, AX = mybir.AluOpType, mybir.ActivationFunctionType, mybir.AxisListType

    adj_t = adj.rearrange("(g p t) m -> g t p m", g=NG, p=P)
    x_g = x.rearrange("(g p t) f -> g p t f", g=NG, p=P)
    out_g = out.rearrange("(g p t) f -> g p t f", g=NG, p=P)

    ctx = ExitStack()
    with ctx:
        def sb(name, shape, dt):
            return ctx.enter_context(nc.sbuf_tensor(name, shape, dt))

        def sem(name):
            return ctx.enter_context(nc.semaphore(name))

        mask = sb("mask", [P, RING, H], bf16)
        qn = sb("qn", [P, M], bf16)
        found = sb("found", [P, H], bf16)
        pb = sb("pb", [P, N], fp32)
        ent_sb = sb("ent_sb", [P, NB, FA], fp32)
        x_sb = sb("x_sb", [P, T, F], fp32)
        leaky = sb("leaky", [P, 2, 2 * SR], fp32)
        wts = sb("wts", [P, 2, 2 * SR], fp32)
        diag = sb("diag", [P, 2, T, P], bf16)
        ident = sb("ident", [P, P], bf16)
        wT_sb = sb("wT_sb", [F, F], fp32)
        aT_sb = sb("aT_sb", [F, 2], fp32)
        wa = sb("wa", [F, 2], fp32)
        wa1_rep = sb("wa1_rep", [F, P], fp32)
        wa2_rep = sb("wa2_rep", [F, P], fp32)
        onesf = sb("onesf", [P, P], fp32)
        identf = sb("identf", [P, P], fp32)
        acc_sb = sb("acc_sb", [FA, SR], fp32)
        qcol = sb("qcol", [P, NB], fp32)
        q_hi = sb("q_hi", [P, NB], fp32)
        q_lo = sb("q_lo", [P, NB], fp32)
        pcol = sb("pcol", [P, NT], fp32)
        qm = sb("qm", [P, 2], fp32)
        qg = sb("qg", [P, 2], fp32)
        qrange = sb("qrange", [P, 1], fp32)
        qinv = sb("qinv", [P, 1], fp32)
        qoff = sb("qoff", [P, 1], fp32)
        qmin = sb("qmin", [P, 1], fp32)
        top = sb("top", [P, 2, NT], fp32)
        empty = sb("empty", [P, NT], fp32)
        st = sb("st", [P, 4, T], fp32)
        ent_sum = sb("ent_sum", [P, FA], fp32)
        h = sb("h", [P, T, FA], fp32)
        e = sb("e", [P, T, F], fp32)
        y = sb("y", [P, T, F], fp32)
        rinv = sb("rinv", [P, T], fp32)
        mean = sb("mean", [P, T], fp32)
        var = sb("var", [P, T], fp32)
        rstd = sb("rstd", [P, T], fp32)
        mhalf = sb("mhalf", [P, T], fp32)
        y_out = sb("y_out", [P, T, F], fp32)

        turned = mask[0:F, 2 * T:3 * T, :].rearrange("p t m -> p (t m)").bitcast(fp32)
        xT_sb, entT_sb = turned[:, 0:N], turned[:, N:N + M]

        X = [ctx.enter_context(nc.psum_tensor(f"X{i}", [P, SR], fp32)) for i in range(2)]
        acc = [ctx.enter_context(nc.psum_tensor(f"acc{i}", [FA, 512], fp32)) for i in range(2)]
        S = [ctx.enter_context(nc.psum_tensor(f"S{i}", [P, 512], fp32)) for i in range(2)]

        w_in = sem("w_in")
        xT_in = sem("xT_in")
        entT_in = sem("entT_in")
        ent_in = sem("ent_in")
        adj_in = [sem(f"adj_in{i}") for i in range(AHEAD)]
        x_in = sem("x_in")
        out_done = sem("out_done")
        ident_done = sem("ident_done")
        const_done = sem("const_done")
        wa_mm = sem("wa_mm")
        wa_done = sem("wa_done")
        cols_mm = sem("cols_mm")
        cols_done = sem("cols_done")
        qmax_done = sem("qmax_done")
        q_all = sem("q_all")
        q_step = sem("q_step")
        q_parts = sem("q_parts")
        rep_done = sem("rep_done")
        row_mm = sem("row_mm")
        q_rows = sem("q_rows")
        p_rows = sem("p_rows")
        sum_mm = sem("sum_mm")
        sum_done = sem("sum_done")
        top_done = sem("top_done")
        mask_done = sem("mask_done")
        st_step = sem("st_step")
        diag_done = sem("diag_done")
        x_done = sem("x_done")
        leaky_done = sem("leaky_done")
        z_done = sem("z_done")
        w_done = sem("w_done")
        w_used = sem("w_used")
        acc_free = sem("acc_free")
        sums_done = sem("sums_done")
        sums_free = sem("sums_free")
        ep_step = sem("ep_step")
        neg_done = sem("neg_done")
        exp_done = sem("exp_done")
        var_done = sem("var_done")
        rstd_done = sem("rstd_done")
        y_done = sem("y_done")

        block = ctx.enter_context(nc.Block())
        qneg = top[:, 0, 0:NB]

        def steps(eng, f, body, head=None):
            body(f, 0)
            if head:
                head()
            with eng.Fori(1, V) as v:
                body(f, v)

        def store(sp, g):
            sp.wait_ge(y_done, g + 1)
            sp.dma_start(out_g[g], y_out[:, :, :]).then_inc(out_done, 16)
            if g + 1 < NG:
                sp.dma_start(x_sb[:, :, :], x_g[g + 1]).then_inc(x_in, 16)

        def all_max(pool):
            pool.wait_ge(qmax_done, 2)
            pool.partition_all_reduce(qg[:, :], qm[:, :], P, bass.bass_isa.ReduceOp.max).then_inc(q_all, 1)

        def inverse_std(pool, g):
            pool.wait_ge(var_done, g + 1)
            pool.tensor_tensor(rstd[:, :], var[:, :], mhalf[:, :], ALU.pow).then_inc(rstd_done, 1)

        def elu_exp(act, g):
            act.wait_ge(neg_done, g + 1)
            act.activation(e[:, :, :], e[:, :, :], ACT.Exp).then_inc(exp_done, 1)

        @block.sync
        def _(sp):
            sp.dma_start(wT_sb[:, :], wT).then_inc(w_in, 16)
            sp.dma_start(aT_sb[:, :], aT).then_inc(w_in, 16)
            sp.dma_start(entT_sb, entT).then_inc(entT_in, 16)
            sp.dma_start(xT_sb, xT).then_inc(xT_in, 16)
            sp.dma_start(ent_sb[:, :, 0:F], ent.rearrange("(b p) f -> p b f", p=P)).then_inc(ent_in, 16)
            sp.dma_start(x_sb[:, :, :], x_g[0]).then_inc(x_in, 16)
            for g in range(NG):
                store(sp, g)
            sp.wait_ge(out_done, 16 * NG)

        @block.gpsimd
        def _(pool):
            pool.memset(ident[:, :], 0.0).then_inc(ident_done, 1)
            pool.memset(identf[:, :], 0.0).then_inc(ident_done, 1)
            pool.wait_ge(ident_done, 2)
            pool.affine_select(out=identf[:, :], in_=identf[:, :], compare_op=ALU.not_equal, fill=1.0,
                               base=0, pattern=[[-1, P]], channel_multiplier=1).then_inc(ident_done, 1)
            pool.affine_select(out=ident[:, :], in_=ident[:, :], compare_op=ALU.not_equal, fill=1.0,
                               base=0, pattern=[[-1, P]], channel_multiplier=1).then_inc(ident_done, 1)

            def load(n):
                f, t = n // T, n % T
                if f == 2 and t == 0:
                    pool.wait_ge(cols_mm, 2)
                if n >= RING and (n - RING) % T == 0:
                    pool.wait_ge(x_done, HB * ((n - RING) // T + 1))
                if n >= AHEAD:
                    pool.wait_ge(mask_done, n - AHEAD + 1)
                col = H * (f % 2)
                pool.dma_start(mask[:, n % RING, :], adj_t[f // 2, t, :, col:col + H]).then_inc(adj_in[n % AHEAD], 16)


            for n in range(AHEAD):
                load(n)
            all_max(pool)
            for n in range(AHEAD, PH * T):
                load(n)
                g, late = divmod(n - 5 * T - AHEAD, 2 * T)
                if g >= 0 and late == 0:
                    inverse_std(pool, g)
                    passed = g + 1
            for g in range(passed, NG):
                inverse_std(pool, g)

        @block.scalar
        def _(act):
            for c in range(8):
                act.wait_ge(row_mm, 9 + c)
                act.activation(pb[:, 512 * c:512 * c + 512], S[c % 2][:, :], ACT.Copy).then_inc(p_rows, 1)
            act.wait_ge(p_rows, 8)
            act.wait_ge(q_parts, 1)

            def weights(slot, block):
                for b in range(2):
                    part = wts[:, slot, SR * b:SR * b + SR]
                    act.activation(part, part, ACT.Exp, bias=q_lo[:, bass.ds(block + b, 1)]).then_inc(w_done, 1)

            def scores(f, v):
                for c in range(2):
                    k = HB // 2 * f + 2 * v + c
                    if not (f == 0 and isinstance(v, int)):
                        act.wait_ge(z_done, 2 * k - 2)
                        weights(c, (HB * (f % 2) - 4 + NB) % NB + 2 * c if isinstance(v, int)
                                else HB * (f % 2) + 4 * v + 2 * c - 4)
                    for b in range(2):
                        act.activation(leaky[:, c, SR * b:SR * b + SR], pb[:, SR * (f // 2):SR * (f // 2) + SR],
                                       ACT.Relu, bias=q_hi[:, bass.ds(HB * (f % 2) + 4 * v + 2 * c + b, 1)],
                                       scale=1 - ALPHA).then_inc(leaky_done, 1)

            for f in range(PH):
                steps(act, f, scores)
                if f % 2 == 0 and f >= 2:
                    elu_exp(act, f // 2 - 1)
            for k in range(NP * NG - 2, NP * NG):
                act.wait_ge(z_done, 2 * k + 2)
                weights(k % 2, 2 * (k % NP))
            elu_exp(act, NG - 1)

        @block.vector
        def _(dve):
            dve.memset(onesf[:, :], 1.0)
            dve.memset(mhalf[:, :], -0.5)
            dve.memset(ent_sb[:, :, F:FA], 1.0).then_inc(const_done, 1)
            dve.wait_ge(wa_mm, 1)
            dve.tensor_copy(wa[:, :], S[0][0:F, 0:2]).then_inc(wa_done, 1)
            dve.wait_ge(cols_mm, 1)
            dve.tensor_copy(qcol[:, :], S[1][:, 0:NB]).then_inc(cols_done, 1)
            dve.wait_ge(cols_done, 1)
            dve.tensor_reduce(qm[:, 0:1], qcol[:, :], AX.X, ALU.max).then_inc(qmax_done, 1)
            dve.tensor_scalar(q_hi[:, :], qcol[:, :], 1 - ALPHA, None, ALU.mult)
            dve.tensor_scalar(q_lo[:, :], qcol[:, :], ALPHA, None, ALU.mult).then_inc(q_parts, 1)
            dve.tensor_scalar(qneg, qcol[:, :], -1.0, None, ALU.mult).then_inc(q_step, 1)
            dve.wait_ge(q_step, 1)
            dve.tensor_reduce(qm[:, 1:2], qneg, AX.X, ALU.max).then_inc(qmax_done, 1)
            dve.wait_ge(q_all, 1)
            dve.tensor_scalar(qmin[:, :], qg[:, 1:2], -1.0, None, ALU.mult)
            dve.scalar_tensor_tensor(qrange[:, :], qg[:, 0:1], 1e-3, qg[:, 1:2], ALU.add, ALU.add).then_inc(q_step, 1)
            dve.wait_ge(q_step, 2)
            dve.tensor_scalar(qrange[:, :], qrange[:, :], 1.02, None, ALU.mult).then_inc(q_step, 1)
            dve.wait_ge(q_step, 3)
            dve.reciprocal(qinv[:, :], qrange[:, :]).then_inc(q_step, 1)
            dve.wait_ge(q_step, 4)
            dve.tensor_tensor(qoff[:, :], qg[:, 1:2], qinv[:, :], ALU.mult).then_inc(q_step, 1)
            dve.tensor_scalar(wa2_rep[:, :], onesf[0:F, :], wa[:, 1:2], qinv[0:F, :], ALU.mult,
                              ALU.mult).then_inc(rep_done, 1)
            dve.tensor_scalar(wa1_rep[:, :], onesf[0:F, :], wa[:, 0:1], None, ALU.mult).then_inc(rep_done, 1)
            dve.wait_ge(q_step, 5)
            for c in range(8):
                dve.wait_ge(row_mm, 1 + c)
                dve.tensor_scalar(qn[:, 512 * c:512 * c + 512], S[c % 2][:, :], qoff[:, :], 2.0 ** -7, ALU.add,
                                  ALU.max).then_inc(q_rows, 1)
            dve.wait_ge(q_rows, 8)

            def clamp(n):
                part = mask[:, n % RING, :]
                dve.wait_ge(adj_in[n % AHEAD], 16 * (n // AHEAD + 1))
                dve.tensor_scalar(part, part, 1.0, 0.0, ALU.min, ALU.max).then_inc(mask_done, 1)

            def search(n):
                if n + 1 < PH * T:
                    clamp(n + 1)
                f, t = n // T, n % T
                dve.wait_ge(mask_done, n + 1)
                if n:
                    dve.wait_ge(top_done, n)
                dve.tensor_tensor_reduce(out=found[:, :], in0=mask[:, n % RING, :], in1=qn[:, H * (f % 2):H * (f % 2) + H],
                                         scale=1.0, scalar=0.0, op0=ALU.mult, op1=ALU.max,
                                         accum_out=top[:, f % 2, T * (f // 2) + t:T * (f // 2) + t + 1]).then_inc(top_done, 1)

            def make_diag(g):
                s = slice(T * g, T * g + T)
                n = 6 * g
                dve.wait_ge(top_done, 2 * T * (g + 1))
                dve.tensor_tensor(st[:, 3], top[:, 0, s], top[:, 1, s], ALU.max).then_inc(st_step, 1)
                dve.wait_ge(st_step, n + 1)
                dve.tensor_scalar(empty[:, s], st[:, 3], 0.0, None, ALU.is_le)
                dve.tensor_scalar(st[:, 0], st[:, 3], qrange[:, :], qmin[:, :], ALU.mult, ALU.add).then_inc(st_step, 1)
                dve.wait_ge(st_step, n + 2)
                dve.tensor_tensor(st[:, 1], st[:, 0], pcol[:, s], ALU.add).then_inc(st_step, 1)
                dve.wait_ge(st_step, n + 3)
                dve.tensor_scalar(st[:, 2], st[:, 1], 0.0, 1 - ALPHA, ALU.max, ALU.mult).then_inc(st_step, 1)
                dve.wait_ge(st_step, n + 4)
                dve.scalar_tensor_tensor(st[:, 2], st[:, 0], ALPHA, st[:, 2], ALU.mult, ALU.add).then_inc(st_step, 1)
                dve.wait_ge(st_step, n + 5)
                dve.tensor_scalar(st[:, 3], st[:, 2], -1.0, BIG, ALU.mult, ALU.add).then_inc(st_step, 1)
                dve.wait_ge(st_step, n + 6)
                dve.tensor_tensor(diag[:, g % 2], ident[:, :].unsqueeze(1).to_broadcast([P, T, P]),
                                  st[:, 3].unsqueeze(2).to_broadcast([P, T, P]), ALU.mult).then_inc(diag_done, 1)

            def exponents(k):
                for b in range(2):
                    if k >= 2:
                        dve.wait_ge(w_used, 2 * k - 3 + b)
                    dve.wait_ge(x_done, 2 * k + b + 1)
                    dve.wait_ge(leaky_done, 2 * k + b + 1)
                    dve.scalar_tensor_tensor(wts[:, k % 2, SR * b:SR * b + SR], X[b][:, :], -BIG,
                                             leaky[:, k % 2, SR * b:SR * b + SR], ALU.add, ALU.add).then_inc(z_done, 1)

            def phase(f):
                for t in range(T):
                    if f + 2 < PH:
                        search(T * (f + 2) + t)
                        if f % 2 == 1 and t == T - 1:
                            make_diag(f // 2 + 1)
                    if f % 2 == 0 and f >= 2 and t == 2:
                        take_acc(f // 2 - 1)
                    exponents(HB // 2 * f + t)
                    if f % 2 == 0 and f >= 2 and t == 3:
                        take_sums(f // 2 - 1)
                        attend(f // 2 - 1)
                if f % 2 == 0 and f >= 2:
                    finish(f // 2 - 1)

            def take_acc(g):
                dve.wait_ge(w_used, NB * g + NB)
                if g:
                    dve.wait_ge(sums_done, g)
                for a in range(2):
                    ins = dve.tensor_copy(acc_sb[:, 512 * a:512 * a + 512], acc[a][:, :])
                ins.then_inc(acc_free, 1)

            def take_sums(g):
                dve.wait_ge(sums_done, g + 1)
                for t in range(T):
                    ins = dve.scalar_tensor_tensor(h[:, t, :], ent_sum[:, :], empty[:, T * g + t:T * g + t + 1],
                                                   S[t // (T // 2)][:, FA * (t % (T // 2)):FA * (t % (T // 2)) + FA],
                                                   ALU.mult, ALU.add)
                ins.then_inc(sums_free, 1)

            chained = [0]

            def chain(ins):
                chained[0] += 1
                ins.then_inc(ep_step, 1)
                dve.wait_ge(ep_step, chained[0])

            def spread(a):
                return a[:, :].unsqueeze(2).to_broadcast([P, T, F])

            def attend(g):
                dve.wait_ge(sums_free, g + 1)
                dve.wait_ge(x_in, 16 * (g + 1))
                chain(dve.reciprocal(rinv[:, :], h[:, :, F]))
                chain(dve.tensor_tensor(y[:, :, :], h[:, :, 0:F], spread(rinv), ALU.mult))
                chain(dve.tensor_tensor(y[:, :, :], y[:, :, :], x_sb[:, :, :], ALU.add))
                dve.tensor_scalar(e[:, :, :], y[:, :, :], 0.0, None, ALU.min).then_inc(neg_done, 1)
                chain(dve.scalar_tensor_tensor(y[:, :, :], y[:, :, :], 0.0, x_sb[:, :, :], ALU.max, ALU.add))

            def finish(g):
                dve.wait_ge(exp_done, g + 1)
                chain(dve.scalar_tensor_tensor(y[:, :, :], e[:, :, :], -1.0, y[:, :, :], ALU.add, ALU.add))
                chain(dve.tensor_reduce(mean[:, :], y[:, :, :], AX.X, ALU.add))
                chain(dve.tensor_scalar(mean[:, :], mean[:, :], 1.0 / F, None, ALU.mult))
                chain(dve.tensor_tensor(y[:, :, :], y[:, :, :], spread(mean), ALU.subtract))
                chain(dve.tensor_tensor(e[:, :, :], y[:, :, :], y[:, :, :], ALU.mult))
                chain(dve.tensor_reduce(var[:, :], e[:, :, :], AX.X, ALU.add))
                dve.tensor_scalar(var[:, :], var[:, :], 1.0 / F, EPS, ALU.mult, ALU.add).then_inc(var_done, 1)
                dve.wait_ge(rstd_done, g + 1)
                if g >= 1:
                    dve.wait_ge(out_done, 16 * g)
                dve.tensor_tensor(y_out[:, :, :], y[:, :, :], spread(rstd), ALU.mult).then_inc(y_done, 1)

            clamp(0)
            for n in range(2 * T):
                search(n)
            dve.wait_ge(cols_mm, 2)
            dve.tensor_copy(pcol[:, :], S[1][:, NB:NB + NT]).then_inc(cols_done, 1)
            dve.wait_ge(sum_mm, 1)
            dve.tensor_copy(ent_sum[:, :], S[0][:, 0:FA]).then_inc(sum_done, 1)
            dve.wait_ge(cols_done, 2)
            dve.wait_ge(sum_done, 1)
            make_diag(0)
            for f in range(PH):
                phase(f)
            take_acc(NG - 1)
            take_sums(NG - 1)
            attend(NG - 1)
            finish(NG - 1)

        @block.tensor
        def _(pe):
            pe.wait_ge(w_in, 32)
            pe.matmul(S[0][0:F, 0:2], wT_sb[:, :], aT_sb[:, :], start=True, stop=True).then_inc(wa_mm, 1)
            pe.wait_ge(wa_done, 1)
            pe.wait_ge(entT_in, 16)
            for b in range(NB):
                ins = pe.matmul(S[1][:, b:b + 1], entT_sb[:, P * b:P * b + P], wa[:, 1:2], start=True, stop=True)
            ins.then_inc(cols_mm, 1)
            pe.wait_ge(rep_done, 1)
            pe.wait_ge(cols_done, 1)
            for c in range(8):
                if c >= 2:
                    pe.wait_ge(q_rows, c - 1)
                pe.matmul(S[c % 2][:, :], wa2_rep[:, :], entT_sb[:, 512 * c:512 * c + 512],
                          start=True, stop=True).then_inc(row_mm, 1)
            pe.wait_ge(rep_done, 2)
            pe.wait_ge(xT_in, 16)
            for c in range(8):
                if c < 2:
                    pe.wait_ge(q_rows, 7 + c)
                else:
                    pe.wait_ge(p_rows, c - 1)
                pe.matmul(S[c % 2][:, :], wa1_rep[:, :], xT_sb[:, 512 * c:512 * c + 512],
                          start=True, stop=True).then_inc(row_mm, 1)
            pe.wait_ge(p_rows, 8)
            for t in range(NT):
                ins = pe.matmul(S[1][:, NB + t:NB + t + 1], xT_sb[:, P * t:P * t + P], wa[:, 0:1], start=True, stop=True)
            ins.then_inc(cols_mm, 1)
            pe.wait_ge(ent_in, 16)
            pe.wait_ge(const_done, 1)
            for b in range(NB):
                ins = pe.matmul(S[0][:, 0:FA], onesf[:, :], ent_sb[:, b, :], start=(b == 0), stop=(b == NB - 1))
            ins.then_inc(sum_mm, 1)
            pe.wait_ge(ident_done, 4)

            def turn(i):
                f = i // HB
                if i >= 2:
                    pe.wait_ge(z_done, i - 1)
                for t in range(T):
                    ins = pe.matmul(X[i % 2][:, P * t:P * t + P], mask[:, (T * f + t) % RING, P * (i % HB):P * (i % HB) + P],
                                    diag[:, f // 2 % 2, t, :], start=True, stop=True)
                ins.then_inc(x_done, 1)

            def weigh(i):
                pe.wait_ge(w_done, i + 1)
                for a in range(2):
                    ins = pe.matmul(acc[a][:, :], ent_sb[:, i % NB, :], wts[:, i // 2 % 2, SR * (i % 2) + 512 * a:SR * (i % 2) + 512 * a + 512],
                                    start=(i % NB == 0), stop=(i % NB == NB - 1))
                ins.then_inc(w_used, 1)

            def turn_back(g):
                pe.wait_ge(acc_free, g + 1)
                if g:
                    pe.wait_ge(sums_free, g)
                for t in range(T):
                    ins = pe.transpose(S[t // (T // 2)][:, FA * (t % (T // 2)):FA * (t % (T // 2)) + FA],
                                       acc_sb[:, P * t:P * t + P], identf[0:FA, 0:FA])
                ins.then_inc(sums_done, 1)

            for i in range(NB * NG + 4):
                if i < NB * NG:
                    if i % NB == 0:
                        pe.wait_ge(diag_done, i // NB + 1)
                    turn(i)
                if i >= 4:
                    if i % NB == 4 and i > 4:
                        turn_back(i // NB - 1)
                    weigh(i - 4)
            turn_back(NG - 1)


def kernel(x, adj, L0_gnn_entity_embs, L0_gnn_W, L0_gnn_a):
    import concourse.bacc as bacc
    from concourse.bass_utils import run_bass_kernel_spmd

    x, adj, ent = np.asarray(x), np.asarray(adj), np.asarray(L0_gnn_entity_embs)
    w, a = np.asarray(L0_gnn_W), np.asarray(L0_gnn_a)
    xT = x.reshape(NG, P, T, F).transpose(3, 0, 2, 1).reshape(F, N)
    arrays = {"x": x, "adj": adj, "ent": ent, "xT": xT, "entT": ent.T, "wT": w.T, "aT": a.reshape(2, F).T}
    arrays = {k: np.ascontiguousarray(v) for k, v in arrays.items()}
    nc = bacc.Bacc("TRN2", target_bir_lowering=False, num_devices=1)
    args = {k: nc.dram_tensor(f"{k}_dram", v.shape, mybir.dt.from_np(v.dtype), kind="ExternalInput").ap()
            for k, v in arrays.items()}
    out = nc.dram_tensor("out_dram", (N, F), mybir.dt.float32, kind="ExternalOutput").ap()
    attention_layernorm(nc, **args, out=out)
    r = run_bass_kernel_spmd(nc, [{f"{k}_dram": v for k, v in arrays.items()}], core_ids=[0])
    return r.results[0]["out_dram"]
```

```python
import numpy as np
import concourse.bass as bass
from concourse import mybir
from contextlib import ExitStack

P = 128
N, M, F = 4096, 4096, 64
SIZES = (5, 8, 8, 7, 4)
T = max(SIZES)
NG = len(SIZES)
TILE0 = [sum(SIZES[:g]) for g in range(NG)]
NT = N // P
NB = M // P
H = M // 2
HB = NB // 2
HALVES = [(g, f, t) for g in range(NG) for f in range(2) for t in range(SIZES[g])]
RING = 26
AHEAD = 4
SLOTS = 5
PARTS = 6
SUM_BLOCKS = 7
FIRST_BY_ACT = 5
LEAKY_AHEAD = 3
ACC_AT = LEAKY_AHEAD + 1
SUMS_AT = 8
ELU_AT = 16
TURNED = 4
LEAKY_EACH = 4
LAG = 3
FA = F + 1
ALPHA = 0.2
BIG = 8192.0
EPS = 1e-5


def attention_layernorm(nc, x, adj, ent_blocks, turned_in, weights_in, out):
    fp32, bf16 = mybir.dt.float32, mybir.dt.bfloat16
    ALU, ACT, AX = mybir.AluOpType, mybir.ActivationFunctionType, mybir.AxisListType

    def rows(a, g):
        part = a[P * TILE0[g]:P * (TILE0[g] + SIZES[g]), :]
        return part.rearrange("(p t) m -> p t m", p=P)


    ctx = ExitStack()
    with ctx:
        def sb(name, shape, dt):
            return ctx.enter_context(nc.sbuf_tensor(name, shape, dt))

        def sem(name):
            return ctx.enter_context(nc.semaphore(name))

        mask = sb("mask", [P, RING, H], bf16)
        qn = sb("qn", [P, M], bf16)
        found = sb("found", [P, H], bf16)
        pb = sb("pb", [P, N], fp32)
        ent_sb = sb("ent_sb", [P, NB, FA], fp32)
        x_sb = sb("x_sb", [P, T, F], fp32)
        leaky = sb("leaky", [P, SLOTS, P * T], fp32)
        wts = sb("wts", [P, SLOTS, P * T], fp32)
        diag = sb("diag", [P, 2, T, P], bf16)
        ident = sb("ident", [P, P], bf16)
        w_sb = sb("w_sb", [F, 2 * F + 2], fp32)
        a_rep = sb("a_rep", [F, 2, P], fp32)
        wa_rep = sb("wa_rep", [P, 2, P], fp32)
        wa2_row = sb("wa2_row", [P, F], fp32)
        onesf = sb("onesf", [P, P], fp32)
        identf = sb("identf", [P, P], fp32)
        acc_sb = sb("acc_sb", [FA, P * T], fp32)
        qcol = sb("qcol", [P, NB], fp32)
        q_hi = sb("q_hi", [P, NB], fp32)
        q_lo = sb("q_lo", [P, NB], fp32)
        pcol = sb("pcol", [P, NT], fp32)
        qm = sb("qm", [P, 2], fp32)
        qg = sb("qg", [P, 2], fp32)
        margin = sb("margin", [P, 1], fp32)
        qabs = sb("qabs", [P, 1], fp32)
        qrange = sb("qrange", [P, 1], fp32)
        qmin_neg = sb("qmin_neg", [P, 1], fp32)
        qmin = sb("qmin", [P, 1], fp32)
        qinv = sb("qinv", [P, 1], fp32)
        qoff = sb("qoff", [P, 1], fp32)
        top = sb("top", [P, 2, NT], fp32)
        empty = sb("empty", [P, NT], fp32)
        st = sb("st", [P, 4, T], fp32)
        ent_sum = sb("ent_sum", [P, FA], fp32)
        h = sb("h", [P, T, FA], fp32)
        e = sb("e", [P, T, F], fp32)
        y = sb("y", [P, T, F], fp32)
        total = sb("total", [P, T], fp32)
        minus1 = sb("minus1", [P, T], fp32)
        mean = sb("mean", [P, T], fp32)
        var = sb("var", [P, T], fp32)
        rstd = sb("rstd", [P, T], fp32)
        mhalf = sb("mhalf", [P, T], fp32)
        y_out = sb("y_out", [P, T, F], fp32)

        ent_wa2 = wts[:, 0:2, :].rearrange("p s (b f) -> p (s b) f", f=F)

        turned = mask[:, RING - TURNED:RING, :].rearrange("p t m -> p (t m)").bitcast(fp32)

        X = [ctx.enter_context(nc.psum_tensor(f"X{i}", [P, P * T], fp32)) for i in range(3)]
        acc = [ctx.enter_context(nc.psum_tensor(f"acc{i}", [P, 512], fp32)) for i in range(2)]
        bank = [X[i][:, 512 * k:512 * k + 512] for i in range(3) for k in range(2)] + [a[:, :] for a in acc]

        w_in = sem("w_in")
        cols_in = [sem(f"cols_in{k}") for k in range(2)]
        ent_in = sem("ent_in")
        adj_in = [sem(f"adj_in{i}") for i in range(AHEAD)]
        x_in = sem("x_in")
        out_done = sem("out_done")
        ident_done = sem("ident_done")
        const_done = sem("const_done")
        wa_zero = sem("wa_zero")
        wa_mm = sem("wa_mm")
        wa_done = sem("wa_done")
        rep_done = sem("rep_done")
        qcol_step = sem("qcol_step")
        qmax_done = sem("qmax_done")
        q_all = sem("q_all")
        q_step = sem("q_step")
        q_parts = sem("q_parts")
        scale_done = sem("scale_done")
        q_mm = sem("q_mm")
        p_mm = sem("p_mm")
        q_lo_rows = sem("q_lo_rows")
        q_hi_rows = sem("q_hi_rows")
        p_rows = sem("p_rows")
        pcol_mm = sem("pcol_mm")
        pcol_done = sem("pcol_done")
        sum_mm = sem("sum_mm")
        sum_done = sem("sum_done")
        top_done = sem("top_done")
        dve_mask_done = sem("dve_mask_done")
        act_mask_done = sem("act_mask_done")
        st_step = sem("st_step")
        diag_done = sem("diag_done")
        x_done = sem("x_done")
        leaky_done = sem("leaky_done")
        leaky_dve_done = sem("leaky_dve_done")
        z_done = sem("z_done")
        w_done = sem("w_done")
        w_used = sem("w_used")
        acc_free = sem("acc_free")
        sums_done = sem("sums_done")
        sums_free = sem("sums_free")
        ep_step = sem("ep_step")
        att_done = sem("att_done")
        elu_step = sem("elu_step")
        elu_done = sem("elu_done")
        y_done = sem("y_done")
        last_step = sem("last_step")
        last_att_done = sem("last_att_done")
        last_elu_done = sem("last_elu_done")
        last_var_done = sem("last_var_done")
        last_rstd_done = sem("last_rstd_done")
        last_done = sem("last_done")

        block = ctx.enter_context(nc.Block())
        SUMS = LAG + 3

        passes = []
        for g in range(NG):
            passes += [(g, b) for b in range(SUMS)] + [(g - 1, None)] * (g > 0) + [(g, b) for b in range(SUMS, NB)]
        passes.append((NG - 1, None))
        place = {at: n for n, at in enumerate(passes)}

        def slot(g, b):
            return X[place[g, b] % len(X)]

        def searched(g, b):
            return 0 if g + 1 == NG else -(-(b + 1) * 2 * SIZES[g + 1] // NB)

        qneg = top[:, 0, 0:NB]

        def sums_at(t):
            return slice(512 * (t // 4) + FA * (t % 4), 512 * (t // 4) + FA * (t % 4) + FA)

        def cols(g):
            return P * SIZES[g]

        def acc_parts(g):
            return [(a, min(512, cols(g) - 512 * a)) for a in range(-(-cols(g) // 512))]

        def by_act(n):
            g = HALVES[n][0]
            if g == 0:
                return n >= FIRST_BY_ACT
            if g == 1:
                return n % 2 == 1
            return g < NG - 1 and n % 4 == 3

        def leaky_by_dve(g, b):
            return g == NG - 1 or g == NG - 2 and b % LEAKY_EACH == LEAKY_EACH - 1

        def leaky_of(dve_ones, g, b):
            return sum(leaky_by_dve(k // NB, k % NB) == dve_ones for k in range(NB * g + b + 1))

        def masks_of(act_ones, n):
            return sum(by_act(m) == act_ones for m in range(n + 1))

        def mask_made(engine, n):
            engine.wait_ge(act_mask_done if by_act(n) else dve_mask_done, masks_of(by_act(n), n))

        def blocks_before(n):
            g, f, _ = HALVES[n]
            return NB * g + HB * (f + 1)

        def halves_before(g):
            return 2 * TILE0[g]

        @block.sync
        def _(sp):
            sp.dma_start(w_sb[:, :], weights_in).then_inc(w_in, 16)
            sp.dma_start(ent_sb[:, :, 0:F], ent_blocks).then_inc(ent_in, 16)
            for k in range(2):
                sp.dma_start(turned[:, H * k:H * k + H], turned_in[:, H * k:H * k + H]).then_inc(cols_in[k], 16)
            sp.dma_start(x_sb[:, 0:SIZES[0], :], rows(x, 0)).then_inc(x_in, 16)
            for g in range(NG):
                if g < NG - 1:
                    sp.wait_ge(y_done, g + 1)
                else:
                    sp.wait_ge(last_done, 1)
                sp.dma_start(rows(out, g), y_out[:, 0:SIZES[g], :]).then_inc(out_done, 16)
                if g + 1 < NG:
                    sp.dma_start(x_sb[:, 0:SIZES[g + 1], :], rows(x, g + 1)).then_inc(x_in, 16)
            sp.wait_ge(out_done, 16 * NG)

        @block.gpsimd
        def _(pool):
            pool.memset(ident[:, :], 0.0).then_inc(ident_done, 1)
            pool.memset(identf[:, :], 0.0).then_inc(ident_done, 1)
            pool.memset(minus1[:, :], -1.0).then_inc(ident_done, 1)
            pool.wait_ge(ident_done, 3)
            pool.affine_select(out=identf[:, :], in_=identf[:, :], compare_op=ALU.not_equal, fill=1.0,
                               base=0, pattern=[[-1, P]], channel_multiplier=1).then_inc(ident_done, 1)
            pool.affine_select(out=ident[:, :], in_=ident[:, :], compare_op=ALU.not_equal, fill=1.0,
                               base=0, pattern=[[-1, P]], channel_multiplier=1).then_inc(ident_done, 1)

            def load(n):
                g, f, t = HALVES[n]
                if n == RING - TURNED:
                    pool.wait_ge(pcol_mm, 2)
                if n >= RING and (n == RING or blocks_before(n - RING) != blocks_before(n - RING - 1)):
                    pool.wait_ge(x_done, blocks_before(n - RING))
                if n >= AHEAD:
                    mask_made(pool, n - AHEAD)
                pool.dma_start(mask[:, n % RING, :], rows(adj, g)[:, t, H * f:H * f + H]).then_inc(adj_in[n % AHEAD], 16)

            chained = [0]

            def chain(ins):
                chained[0] += 1
                ins.then_inc(ep_step, 1)
                pool.wait_ge(ep_step, chained[0])

            def add_up(to_sum, src, n):
                width = F // 2
                while width:
                    to = e[:, 0:n, 0:width] if width > 1 else to_sum[:, 0:n].unsqueeze(2)
                    chain(pool.tensor_tensor(to, src[:, 0:n, 0:width], src[:, 0:n, width:2 * width], ALU.add))
                    src, width = e, width // 2

            def finish(g, part):
                n = SIZES[g]
                y_g, e_g, x_gr = y[:, 0:n, :], e[:, 0:n, :], x_sb[:, 0:n, :]
                small = lambda a: a[:, 0:n]
                spread = lambda a: a[:, 0:n].unsqueeze(2).to_broadcast([P, n, F])
                if part == 0:
                    h_g, none = h[:, 0:n, 0:F], empty[:, TILE0[g]:TILE0[g] + n]
                    pool.wait_ge(diag_done, g + 1)
                    pool.wait_ge(sum_done, 1)
                    chain(pool.tensor_tensor(e_g, ent_sum[:, 0:F].unsqueeze(1).to_broadcast([P, n, F]),
                                             none.unsqueeze(2).to_broadcast([P, n, F]), ALU.mult))
                    chain(pool.tensor_scalar(small(total), none, float(M), 0.0, ALU.mult, ALU.add))
                    pool.wait_ge(sums_free, g + 1)
                    chain(pool.tensor_tensor(small(total).unsqueeze(2), small(total).unsqueeze(2), h[:, 0:n, F:FA], ALU.add))
                    chain(pool.tensor_tensor(h_g, h_g, e_g, ALU.add))
                    pool.wait_ge(x_in, 16 * (g + 1))
                    chain(pool.tensor_tensor(small(total), small(total), small(minus1), ALU.pow))
                    chain(pool.tensor_tensor(y_g, h_g, spread(total), ALU.mult))
                    pool.tensor_tensor(y_g, y_g, x_gr, ALU.add).then_inc(att_done, 1)
                elif part == 1:
                    pool.wait_ge(elu_done, g + 1)
                    chain(pool.tensor_tensor(y_g, y_g, e_g, ALU.add))
                    chain(pool.tensor_tensor(y_g, y_g, x_gr, ALU.add))
                elif part == 2:
                    add_up(mean, y, n)
                    chain(pool.tensor_scalar(small(mean), small(mean), 1.0 / F, 0.0, ALU.mult, ALU.add))
                elif part == 3:
                    chain(pool.tensor_tensor(y_g, y_g, spread(mean), ALU.subtract))
                    chain(pool.tensor_tensor(e_g, y_g, y_g, ALU.mult))
                elif part == 4:
                    add_up(var, e, n)
                    chain(pool.tensor_scalar(small(var), small(var), 1.0 / F, EPS, ALU.mult, ALU.add))
                    chain(pool.tensor_tensor(small(rstd), small(var), small(mhalf), ALU.pow))
                else:
                    if g >= 1:
                        pool.wait_ge(out_done, 16 * g)
                    pool.tensor_tensor(y_out[:, 0:n, :], y_g, spread(rstd), ALU.mult).then_inc(y_done, 1)

            pool.wait_ge(w_in, 16)
            pool.wait_ge(ent_in, 16)
            for n in range(AHEAD):
                load(n)
            pool.wait_ge(qmax_done, 2)
            pool.partition_all_reduce(qg[:, :], qm[:, :], P, bass.bass_isa.ReduceOp.max).then_inc(q_all, 1)
            parts = []
            for g in range(NG - 1):
                first = halves_before(g + 2) + searched(g + 1, SUMS) - 1 + AHEAD if g + 2 < NG else len(HALVES)
                parts += [(first + (part and part + 1), g, part) for part in range(PARTS)]
            for n in range(AHEAD, len(HALVES)):
                load(n)
                while parts[0][0] == n:
                    finish(*parts.pop(0)[1:])
            for _, g, part in parts:
                finish(g, part)
            n = SIZES[NG - 1]
            pool.wait_ge(last_var_done, 1)
            pool.tensor_tensor(rstd[:, 0:n], var[:, 0:n], mhalf[:, 0:n], ALU.pow).then_inc(last_rstd_done, 1)

        @block.scalar
        def _(act):
            act.wait_ge(const_done, 2)
            act.activation(rstd[:, :], mhalf[:, :], ACT.Exp)
            act.wait_ge(scale_done, 1)
            for c in range(4, 8):
                act.wait_ge(q_mm, c + 1)
                act.activation(qn[:, 512 * c:512 * c + 512], bank[c], ACT.Identity, bias=qoff[:, :],
                               scale=qinv[:, :]).then_inc(q_hi_rows, 1)
            for c in range(8):
                act.wait_ge(p_mm, c + 1)
                act.activation(pb[:, 512 * c:512 * c + 512], bank[c], ACT.Copy,
                               scale=1 - ALPHA).then_inc(p_rows, 1)
            act.wait_ge(p_rows, 8)
            act.wait_ge(q_parts, 1)

            def signs(n):
                part = mask[:, n % RING, :]
                act.wait_ge(adj_in[n % AHEAD], 16 * (n // AHEAD + 1))
                act.activation(part, part, ACT.Sign).then_inc(act_mask_done, 1)

            def weights(g, b):
                part = wts[:, (NB * g + b) % SLOTS, 0:cols(g)]
                act.wait_ge(z_done, NB * g + b + 1)
                act.activation(part, part, ACT.Exp, bias=q_lo[:, b:b + 1]).then_inc(w_done, 1)

            def relus(g, b):
                act.activation(leaky[:, (NB * g + b) % SLOTS, 0:cols(g)], pb[:, P * TILE0[g]:P * TILE0[g] + cols(g)],
                               ACT.Relu, bias=q_hi[:, b:b + 1]).then_inc(leaky_done, 1)

            def elu(g):
                y_g, e_g = y[:, 0:SIZES[g], :], e[:, 0:SIZES[g], :]
                act.wait_ge(att_done, g + 1)
                act.activation(e_g, y_g, ACT.Relu, scale=-1.0).then_inc(elu_step, 1)
                act.wait_ge(elu_step, 2 * g + 1)
                act.activation(e_g, e_g, ACT.Exp, scale=-1.0).then_inc(elu_step, 1)
                act.activation(y_g, y_g, ACT.Relu)
                act.wait_ge(elu_step, 2 * g + 2)
                act.activation(e_g, e_g, ACT.Copy, bias=-1.0).then_inc(elu_done, 1)

            def take_acc(g):
                act.wait_ge(w_used, NB * g + NB)
                if g:
                    act.wait_ge(sums_done, g)
                for a, n in acc_parts(g):
                    ins = act.activation(acc_sb[:, 512 * a:512 * a + n], acc[a][0:FA, 0:n], ACT.Copy)
                ins.then_inc(acc_free, 1)

            def take_sums(g):
                act.wait_ge(sums_done, g + 1)
                for k in range(0, SIZES[g], 4):
                    n = min(4, SIZES[g] - k)
                    ins = act.activation(h[:, k:k + n, :].rearrange("p t f -> p (t f)"),
                                         slot(g, None)[:, 128 * k:128 * k + FA * n], ACT.Copy)
                ins.then_inc(sums_free, 1)

            for n in range(halves_before(1)):
                if by_act(n):
                    signs(n)
            for g in range(NG):
                for b in range(NB):
                    if g and b == ACC_AT:
                        take_acc(g - 1)
                    if g and b == SUMS_AT:
                        take_sums(g - 1)
                    if g and b == ELU_AT:
                        elu(g - 1)
                    for n in range(searched(g, b - 1), searched(g, b)):
                        if by_act(halves_before(g + 1) + n):
                            signs(halves_before(g + 1) + n)
                    if b >= LEAKY_AHEAD:
                        weights(g, b - LEAKY_AHEAD)
                    elif g:
                        weights(g - 1, NB + b - LEAKY_AHEAD)
                    if not leaky_by_dve(g, b):
                        relus(g, b)
            for b in range(NB - LEAKY_AHEAD, NB):
                weights(NG - 1, b)
            take_acc(NG - 1)
            act.wait_ge(last_att_done, 1)
            e_last = e[:, 0:SIZES[NG - 1], :]
            act.activation(e_last, e_last, ACT.Exp).then_inc(last_elu_done, 1)

        @block.vector
        def _(dve):
            def clamp(n):
                part = mask[:, n % RING, :]
                dve.wait_ge(adj_in[n % AHEAD], 16 * (n // AHEAD + 1))
                dve.tensor_scalar(part, part, 1.0, 0.0, ALU.min, ALU.max).then_inc(dve_mask_done, 1)

            dve.memset(onesf[:, :], 1.0).then_inc(const_done, 1)
            dve.memset(mhalf[:, :], -0.5).then_inc(const_done, 1)
            dve.memset(wa_rep[:, :, :], 0.0).then_inc(wa_zero, 1)
            dve.memset(ent_sb[:, :, F:FA], 1.0).then_inc(const_done, 1)
            dve.wait_ge(const_done, 1)
            dve.wait_ge(w_in, 16)
            dve.tensor_tensor(a_rep[:, :, :], onesf[0:F, :].unsqueeze(1).to_broadcast([F, 2, P]),
                              w_sb[:, 2 * F:2 * F + 2].unsqueeze(2).to_broadcast([F, 2, P]), ALU.mult).then_inc(rep_done, 1)
            dve.wait_ge(wa_mm, 1)
            dve.wait_ge(wa_zero, 1)
            dve.tensor_copy(wa_rep[0:F, 0, :], bank[0][0:F, P:2 * P]).then_inc(wa_done, 1)
            dve.tensor_copy(wa_rep[F:2 * F, 1, :], bank[0][F:2 * F, 0:P]).then_inc(wa_done, 1)
            dve.tensor_copy(wa2_row[:, :], bank[0][:, 2 * P:2 * P + F]).then_inc(wa_done, 1)
            dve.wait_ge(wa_done, 3)
            dve.wait_ge(ent_in, 16)
            dve.tensor_tensor(ent_wa2[:, :, :], ent_sb[:, :, 0:F], wa2_row[:, :].unsqueeze(1).to_broadcast([P, NB, F]),
                              ALU.mult).then_inc(qcol_step, 1)
            dve.wait_ge(qcol_step, 1)
            dve.tensor_reduce(qcol[:, :], ent_wa2[:, :, :], AX.X, ALU.add).then_inc(qcol_step, 1)
            dve.wait_ge(qcol_step, 2)
            dve.tensor_reduce(qm[:, 0:1], qcol[:, :], AX.X, ALU.max).then_inc(qmax_done, 1)
            dve.tensor_scalar(qneg, qcol[:, :], -1.0, None, ALU.mult).then_inc(q_step, 1)
            dve.wait_ge(q_step, 1)
            dve.tensor_reduce(qm[:, 1:2], qneg, AX.X, ALU.max).then_inc(qmax_done, 1)
            dve.tensor_scalar(q_hi[:, :], qcol[:, :], 1 - ALPHA, None, ALU.mult)
            dve.tensor_scalar(q_lo[:, :], qcol[:, :], ALPHA, None, ALU.mult).then_inc(q_parts, 1)
            dve.wait_ge(q_all, 1)
            dve.tensor_tensor(qabs[:, :], qg[:, 0:1], qg[:, 1:2], ALU.max)
            dve.tensor_tensor(qrange[:, :], qg[:, 0:1], qg[:, 1:2], ALU.add).then_inc(q_step, 1)
            dve.wait_ge(q_step, 2)
            dve.tensor_scalar(margin[:, :], qrange[:, :], 0.01, 1e-6, ALU.mult, ALU.add).then_inc(q_step, 1)
            dve.wait_ge(q_step, 3)
            dve.scalar_tensor_tensor(margin[:, :], qabs[:, :], 1e-4, margin[:, :], ALU.mult, ALU.add).then_inc(q_step, 1)
            dve.wait_ge(q_step, 4)
            dve.tensor_tensor(qmin_neg[:, :], qg[:, 1:2], margin[:, :], ALU.add)
            dve.scalar_tensor_tensor(qrange[:, :], margin[:, :], 2.0, qrange[:, :], ALU.mult, ALU.add).then_inc(q_step, 1)
            dve.wait_ge(q_step, 5)
            dve.reciprocal(qinv[:, :], qrange[:, :]).then_inc(q_step, 1)
            dve.tensor_scalar(qmin[:, :], qmin_neg[:, :], -1.0, None, ALU.mult)
            dve.wait_ge(q_step, 6)
            dve.tensor_tensor(qoff[:, :], qmin_neg[:, :], qinv[:, :], ALU.mult).then_inc(scale_done, 1)
            clamp(0)
            for i in range(2):
                dve.wait_ge(q_mm, 2 * i + 2)
                dve.tensor_scalar(qn[:, 1024 * i:1024 * i + 1024], X[i][:, :], qmin_neg[:, :], qinv[:, :], ALU.add,
                                  ALU.mult).then_inc(q_lo_rows, 1)
            dve.wait_ge(q_lo_rows, 2)

            def search(n):
                if n + 1 < len(HALVES) and not by_act(n + 1):
                    clamp(n + 1)
                g, f, t = HALVES[n]
                mask_made(dve, n)
                if n:
                    dve.wait_ge(top_done, n)
                dve.tensor_tensor_reduce(out=found[:, :], in0=mask[:, n % RING, :], in1=qn[:, H * f:H * f + H],
                                         scale=1.0, scalar=0.0, op0=ALU.mult, op1=ALU.max,
                                         accum_out=top[:, f, TILE0[g] + t:TILE0[g] + t + 1]).then_inc(top_done, 1)

            def make_diag(g):
                m = SIZES[g]
                s = slice(TILE0[g], TILE0[g] + m)
                n = 6 * g
                dve.wait_ge(top_done, halves_before(g) + 2 * m)
                dve.tensor_tensor(st[:, 3, 0:m], top[:, 0, s], top[:, 1, s], ALU.max).then_inc(st_step, 1)
                dve.wait_ge(st_step, n + 1)
                dve.tensor_scalar(empty[:, s], st[:, 3, 0:m], 0.0, None, ALU.is_le)
                dve.tensor_scalar(st[:, 0, 0:m], st[:, 3, 0:m], qrange[:, :], qmin[:, :], ALU.mult, ALU.add).then_inc(st_step, 1)
                dve.wait_ge(st_step, n + 2)
                dve.tensor_tensor(st[:, 1, 0:m], st[:, 0, 0:m], pcol[:, s], ALU.add).then_inc(st_step, 1)
                dve.wait_ge(st_step, n + 3)
                dve.tensor_scalar(st[:, 2, 0:m], st[:, 1, 0:m], 0.0, 1 - ALPHA, ALU.max, ALU.mult).then_inc(st_step, 1)
                dve.wait_ge(st_step, n + 4)
                dve.scalar_tensor_tensor(st[:, 2, 0:m], st[:, 0, 0:m], ALPHA, st[:, 2, 0:m], ALU.mult, ALU.add).then_inc(st_step, 1)
                dve.wait_ge(st_step, n + 5)
                dve.tensor_scalar(st[:, 3, 0:m], st[:, 2, 0:m], -1.0, BIG, ALU.mult, ALU.add).then_inc(st_step, 1)
                dve.wait_ge(st_step, n + 6)
                dve.tensor_tensor(diag[:, g % 2, 0:m], ident[:, :].unsqueeze(1).to_broadcast([P, m, P]),
                                  st[:, 3, 0:m].unsqueeze(2).to_broadcast([P, m, P]), ALU.mult).then_inc(diag_done, 1)

            def leaky_dve(g, b):
                dve.wait_ge(z_done, NB * g + b - SLOTS + 1)
                dve.tensor_scalar(leaky[:, (NB * g + b) % SLOTS, 0:cols(g)], pb[:, P * TILE0[g]:P * TILE0[g] + cols(g)],
                                  q_hi[:, b:b + 1], 0.0, ALU.add, ALU.max).then_inc(leaky_dve_done, 1)

            def exponents(g, b):
                i, n = NB * g + b, cols(g)
                if i >= SLOTS:
                    dve.wait_ge(w_used, i - SLOTS + 1)
                dve.wait_ge(x_done, i + 1)
                mine = leaky_by_dve(g, b)
                dve.wait_ge(leaky_dve_done if mine else leaky_done, leaky_of(mine, g, b))
                dve.scalar_tensor_tensor(wts[:, i % SLOTS, 0:n], slot(g, b)[:, 0:n], -BIG, leaky[:, i % SLOTS, 0:n],
                                         ALU.add, ALU.add).then_inc(z_done, 1)

            def finish_last():
                g, n = NG - 1, SIZES[NG - 1]
                y_g, e_g, x_gr = y[:, 0:n, :], e[:, 0:n, :], x_sb[:, 0:n, :]
                spread = lambda a: a[:, 0:n].unsqueeze(2).to_broadcast([P, n, F])
                chained = [0]

                def chain(ins):
                    chained[0] += 1
                    ins.then_inc(last_step, 1)
                    dve.wait_ge(last_step, chained[0])

                dve.wait_ge(y_done, g)
                dve.wait_ge(sums_done, g + 1)
                for t in range(n):
                    row = TILE0[g] + t
                    ins = dve.scalar_tensor_tensor(h[:, t, :], ent_sum[:, :], empty[:, row:row + 1],
                                                   slot(g, None)[:, sums_at(t)], ALU.mult, ALU.add)
                chain(ins)
                chain(dve.reciprocal(total[:, 0:n], h[:, 0:n, F]))
                dve.wait_ge(x_in, 16 * (g + 1))
                chain(dve.tensor_tensor(y_g, h[:, 0:n, 0:F], spread(total), ALU.mult))
                chain(dve.tensor_tensor(y_g, y_g, x_gr, ALU.add))
                dve.tensor_scalar(e_g, y_g, 0.0, None, ALU.min).then_inc(last_att_done, 1)
                chain(dve.scalar_tensor_tensor(y_g, y_g, 0.0, x_gr, ALU.max, ALU.add))
                dve.wait_ge(last_elu_done, 1)
                chain(dve.scalar_tensor_tensor(y_g, e_g, -1.0, y_g, ALU.add, ALU.add))
                chain(dve.tensor_reduce(mean[:, 0:n], y_g, AX.X, ALU.add))
                chain(dve.scalar_tensor_tensor(y_g, spread(mean), -1.0 / F, y_g, ALU.mult, ALU.add))
                chain(dve.tensor_tensor(e_g, y_g, y_g, ALU.mult))
                chain(dve.tensor_reduce(var[:, 0:n], e_g, AX.X, ALU.add))
                dve.tensor_scalar(var[:, 0:n], var[:, 0:n], 1.0 / F, EPS, ALU.mult, ALU.add).then_inc(last_var_done, 1)
                dve.wait_ge(last_rstd_done, 1)
                dve.wait_ge(out_done, 16 * g)
                dve.tensor_tensor(y_out[:, 0:n, :], y_g, spread(rstd), ALU.mult).then_inc(last_done, 1)

            def supertile(g):
                if leaky_by_dve(g, 0):
                    leaky_dve(g, 0)
                for b in range(NB):
                    for n in range(searched(g, b - 1), searched(g, b)):
                        search(halves_before(g + 1) + n)
                        if n == 2 * SIZES[g + 1] - 1:
                            make_diag(g + 1)
                    if b + 1 < NB and leaky_by_dve(g, b + 1):
                        leaky_dve(g, b + 1)
                    exponents(g, b)

            for n in range(2 * SIZES[0]):
                if n == SIZES[0]:
                    dve.wait_ge(q_hi_rows, 4)
                search(n)
            dve.wait_ge(pcol_mm, 1)
            dve.tensor_copy(pcol[:, 0:SIZES[0]], acc[0][:, 512 - NT:512 - NT + SIZES[0]]).then_inc(pcol_done, 1)
            dve.wait_ge(pcol_done, 1)
            make_diag(0)
            dve.wait_ge(pcol_mm, 2)
            dve.tensor_copy(pcol[:, SIZES[0]:NT], acc[1][:, 512 - NT + SIZES[0]:512]).then_inc(pcol_done, 1)
            dve.wait_ge(sum_mm, 1)
            dve.tensor_reduce(ent_sum[:, :], acc[1][:, 0:FA * SUM_BLOCKS].rearrange("p (b f) -> p f b", f=FA),
                              AX.X, ALU.add).then_inc(sum_done, 1)
            for g in range(NG):
                supertile(g)
            finish_last()

        @block.tensor
        def _(pe):
            pe.wait_ge(w_in, 16)
            pe.wait_ge(rep_done, 1)
            pe.matmul(bank[0][:, 0:2 * P], w_sb[:, 0:2 * F], a_rep[:, :, :].rearrange("f k m -> f (k m)"),
                      start=True, stop=True)
            pe.matmul(bank[0][:, 2 * P:2 * P + F], a_rep[:, 1, :], w_sb[:, 0:F], start=True, stop=True).then_inc(wa_mm, 1)
            pe.wait_ge(wa_done, 3)
            for c in range(8):
                if c % 4 == 0:
                    pe.wait_ge(cols_in[c // 4], 16)
                pe.matmul(bank[c], wa_rep[:, 0, :], turned[:, 512 * c:512 * c + 512], start=True, stop=True).then_inc(q_mm, 1)
            for c in range(8):
                if c < 4:
                    pe.wait_ge(q_lo_rows, c // 2 + 1)
                else:
                    pe.wait_ge(q_hi_rows, c - 3)
                pe.matmul(bank[c], wa_rep[:, 1, :], turned[:, 512 * c:512 * c + 512], start=True, stop=True).then_inc(p_mm, 1)

            def p_cols(a, first, last):
                for t in range(first, last):
                    ins = pe.matmul(acc[a][:, 512 - NT + t:512 - NT + t + 1], turned[:, P * t:P * t + P],
                                    wa_rep[:, 1, 0:1], start=True, stop=True)
                ins.then_inc(pcol_mm, 1)

            pe.wait_ge(p_rows, 7)
            p_cols(0, 0, SIZES[0])
            pe.wait_ge(p_rows, 8)
            pe.wait_ge(ent_in, 16)
            pe.wait_ge(const_done, 3)
            for b in range(0, NB, SUM_BLOCKS):
                k = min(SUM_BLOCKS, NB - b)
                ins = pe.matmul(acc[1][:, 0:FA * k], onesf[:, :], ent_sb[:, b:b + k, :].rearrange("p b f -> p (b f)"),
                                start=(b == 0), stop=(b + k >= NB))
            ins.then_inc(sum_mm, 1)
            p_cols(1, SIZES[0], NT)
            pe.wait_ge(pcol_done, 1)
            pe.wait_ge(ident_done, 5)

            def slot_free(g, b):
                n = place[g, b] - len(X)
                if n >= 0:
                    before, block = passes[n]
                    if block is None:
                        pe.wait_ge(sums_free, before + 1)
                    else:
                        pe.wait_ge(z_done, NB * before + block + 1)

            def turn(g, b):
                first = halves_before(g) + SIZES[g] * (b // HB)
                slot_free(g, b)
                for t in range(SIZES[g]):
                    ins = pe.matmul(slot(g, b)[:, P * t:P * t + P],
                                    mask[:, (first + t) % RING, P * (b % HB):P * (b % HB) + P],
                                    diag[:, g % 2, t, :], start=True, stop=True)
                ins.then_inc(x_done, 1)

            def weigh(g, b):
                i = NB * g + b
                pe.wait_ge(w_done, i + 1)
                if g and b == 0:
                    pe.wait_ge(acc_free, g)
                for a, n in acc_parts(g):
                    ins = pe.matmul(acc[a][0:FA, 0:n], ent_sb[:, b, :], wts[:, i % SLOTS, 512 * a:512 * a + n],
                                    start=(b == 0), stop=(b == NB - 1))
                ins.then_inc(w_used, 1)

            def turn_back(g):
                pe.wait_ge(acc_free, g + 1)
                slot_free(g, None)
                for t in range(SIZES[g]):
                    ins = pe.transpose(slot(g, None)[:, sums_at(t)],
                                       acc_sb[:, P * t:P * t + P], identf[0:FA, 0:FA])
                ins.then_inc(sums_done, 1)

            for g in range(NG):
                pe.wait_ge(diag_done, g + 1)
                for b in range(NB):
                    turn(g, b)
                    if g and b == SUMS - 1:
                        turn_back(g - 1)
                    if b >= LAG:
                        weigh(g, b - LAG)
                    elif g:
                        weigh(g - 1, NB + b - LAG)
            for b in range(NB - LAG, NB):
                weigh(NG - 1, b)
            turn_back(NG - 1)


def kernel(x, adj, L0_gnn_entity_embs, L0_gnn_W, L0_gnn_a):
    import concourse.bacc as bacc
    from concourse.bass_utils import run_bass_kernel_spmd

    x, adj, ent = np.asarray(x), np.asarray(adj), np.asarray(L0_gnn_entity_embs)
    w, a = np.asarray(L0_gnn_W), np.asarray(L0_gnn_a)
    parts = [x[P * a:P * (a + n)].reshape(P, n, F).transpose(2, 1, 0).reshape(F, P * n) for a, n in zip(TILE0, SIZES)]
    xT = np.concatenate(parts, axis=1)
    ent_blocks = ent.reshape(NB, P, F).transpose(1, 0, 2)
    turned_in = np.concatenate([ent.T, xT], axis=0)
    weights_in = np.concatenate([w.T, w.T, a.reshape(2, F).T], axis=1)
    arrays = {"x": x, "adj": adj, "ent_blocks": ent_blocks, "turned_in": turned_in, "weights_in": weights_in}
    arrays = {k: np.ascontiguousarray(v) for k, v in arrays.items()}
    nc = bacc.Bacc("TRN2", target_bir_lowering=False, num_devices=1)
    args = {k: nc.dram_tensor(f"{k}_dram", v.shape, mybir.dt.from_np(v.dtype), kind="ExternalInput").ap()
            for k, v in arrays.items()}
    out = nc.dram_tensor("out_dram", (N, F), mybir.dt.float32, kind="ExternalOutput").ap()
    attention_layernorm(nc, **args, out=out)
    r = run_bass_kernel_spmd(nc, [{f"{k}_dram": v for k, v in arrays.items()}], core_ids=[0])
    return r.results[0]["out_dram"]
```
